# Optimizing a Trainium2 kernel written in Bass

```python
import numpy as np
import jax
import jax.numpy as jnp

def _softmax(x, axis=-1):
    return jax.nn.softmax(x, axis=axis)

def _gelu(x):
    return jax.nn.gelu(x, approximate=True)

def _silu(x):
    return jax.nn.silu(x)

def _sigmoid(x):
    return jax.nn.sigmoid(x)

def _layernorm(x, axis=-1, eps=1e-05):
    m = jnp.mean(x, axis=axis, keepdims=True)
    v = jnp.var(x, axis=axis, keepdims=True)
    return (x - m) / jnp.sqrt(v + eps)

def _scatter_add(tgt, idx, src, axis=0):
    return tgt.at[idx].add(src)

def _segment_sum(src, seg, n):
    return jax.ops.segment_sum(src, seg, n)
kernel_name = 'mk_rec_standalone_d1_rec_r8_a2f685'

def setup_inputs(seed: int=0):
    np.random.seed(seed)
    _w = jnp.asarray

    def _rec_inputs():
        import jax
        import jax.numpy as jnp
        _rk = jax.random.key(seed)
        r_entity_idxs = jax.random.bernoulli(jax.random.fold_in(_rk, 1), 0.5, (1024, 12500)).astype(jnp.float32)
        return r_entity_idxs
    r_entity_idxs = _rec_inputs()

    def _L0_rec_setup():
        import jax, jax.numpy as jnp
        import numpy as np
        BATCH = 256
        N_ENTITIES = 12500
        LATENT = 128
        key = jax.random.key(seed)
        k1, k2 = jax.random.split(key)
        entity_idxs = jax.random.randint(k1, (BATCH, N_ENTITIES), 0, 2).astype(jnp.float32)
        W = jax.random.normal(k2, (LATENT, N_ENTITIES), dtype=jnp.float32) * (1.0 / np.sqrt(N_ENTITIES))
        return {'entity_idxs': entity_idxs, 'W': W}
    _L0_rec_all = _L0_rec_setup()
    _L0_rec_in = {k: v for k, v in _L0_rec_all.items() if k in ('W',)}
    del _L0_rec_all
    return {'r_entity_idxs': r_entity_idxs, 'L0_rec_W': _L0_rec_in['W']}

def reference(r_entity_idxs, L0_rec_W):
    import jax
    import jax.numpy as jnp

    def _L0_rec_ref(entity_idxs, W):
        import jax, jax.numpy as jnp
        import numpy as np
        BATCH = 256
        N_ENTITIES = 12500
        LATENT = 128
        entities = jnp.einsum('be,le->bl', entity_idxs, W)
        s = jnp.sum(entity_idxs, axis=1)
        s_safe = jnp.where(s != 0, s, 1.0)
        scale = jnp.where(s != 0, 1.0 / s_safe, 1.0)
        return entities * scale[:, None]
    y = _L0_rec_ref(r_entity_idxs, L0_rec_W)
    return y

_drawn_inputs = setup_inputs


def setup_inputs(seed=0):
    import zlib

    import numpy as np

    out = dict(_drawn_inputs(seed))
    spreads = {}
    factors = {}
    for name, (base, spread) in spreads.items():
        noise = np.random.default_rng([zlib.crc32(name.encode()), seed]).standard_normal(out[name].shape)
        drawn = base * np.exp(spread * noise) if base else spread * noise
        out[name] = jnp.asarray(drawn.astype(out[name].dtype))
    for name, factor in factors.items():
        out[name] = (out[name] * factor).astype(out[name].dtype)
    return out
```

```python
from contextlib import ExitStack

import concourse.bass as bass
from concourse import mybir

F32 = mybir.dt.float32
ALU = mybir.AluOpType

P = 128
TILES_PER_BLOCK = 8
CHUNK = 2
SLOTS = 2


def rec_kernel(nc, x_t, w_t, out):
    E, B = x_t.shape
    L = w_t.shape[1]
    T = TILES_PER_BLOCK
    CHUNKS = T // CHUNK
    BLOCKS = E // (P * T)
    PAIRS = BLOCKS // SLOTS
    BT = B // P
    N = L + 1
    main = BLOCKS * P * T
    tail = []
    at = main
    while at < E:
        tail.append((at, min(P, E - at)))
        at += P
    assert BLOCKS % SLOTS == 0 and len(tail) <= T

    x_blocks = x_t[0:main, :].rearrange("(n p j) b -> n p (j b)", p=P, j=T)
    w_blocks = w_t[0:main, :].rearrange("(n p j) l -> n p j l", p=P, j=T)

    with ExitStack() as ctx:
        sb = lambda name, shape, dt: ctx.enter_context(nc.sbuf_tensor(name, shape, dt))
        sem = lambda name: ctx.enter_context(nc.semaphore(name))
        x_sb = sb("x_sb", [P, SLOTS, T, B], F32)
        w_sb = sb("w_sb", [P, SLOTS, T, N], F32)
        scale = sb("scale", [P, BT, 3], F32)
        y = sb("y", [P, BT, L], F32)
        acc = ctx.enter_context(nc.psum_tensor("acc", [P, BT, 512], F32))

        x_in = [[sem(f"x_in_{s}_{c}") for c in range(CHUNKS)] for s in range(SLOTS)]
        w_in = [sem(f"w_in_{s}") for s in range(SLOTS)]
        ones_set = sem("ones_set")
        chunk_used = sem("chunk_used")
        bank_full = sem("bank_full")
        step_done = sem("step_done")
        y_ready = sem("y_ready")
        y_out = sem("y_out")
        block = ctx.enter_context(nc.Block())

        @block.sync
        def _(sp):
            sp.wait_ge(ones_set, 1)

            def load(n, s, c):
                if c == 0:
                    sp.dma_start(w_sb[:, s, :, 0:L], w_blocks[n]).then_inc(w_in[s], 16)
                sp.dma_start(x_sb[:, s, c * CHUNK:(c + 1) * CHUNK, :].rearrange("p j b -> p (j b)"),
                             x_blocks[n, :, c * CHUNK * B:(c + 1) * CHUNK * B]).then_inc(x_in[s][c], 16)

            for s in range(SLOTS):
                for c in range(CHUNKS):
                    load(s, s, c)
            with sp.Fori(1, PAIRS) as i:
                for s in range(SLOTS):
                    for c in range(CHUNKS):
                        sp.wait_ge(chunk_used, ((i - 1) * SLOTS + s) * CHUNKS + (CHUNKS if c == 0 else c + 1))
                        load(i * SLOTS + s, s, c)
            sp.wait_ge(chunk_used, ((PAIRS - 1) * SLOTS + 1) * CHUNKS)
            for k, (row, rows) in enumerate(tail):
                sp.dma_start(w_sb[0:rows, 0, k, 0:L], w_t[row:row + rows, :]).then_inc(x_in[0][k], 16)
                sp.dma_start(x_sb[0:rows, 0, k, :], x_t[row:row + rows, :]).then_inc(x_in[0][k], 16)
            for b in range(BT):
                sp.wait_ge(y_ready, b + 1)
                sp.dma_start(out[b * P:(b + 1) * P, :], y[:, b, :]).then_inc(y_out, 16)
            sp.wait_ge(y_out, 16 * BT)

        @block.tensor
        def _(pe):
            def tile(s, j, rows, first, last):
                for b in range(BT):
                    mm = nc.tensor.matmul(acc[:, b, 0:N], x_sb[0:rows, s, j, b * P:(b + 1) * P],
                                          w_sb[0:rows, s, j, :], start=first, stop=last)
                    if last:
                        mm.then_inc(bank_full, 1)
                return mm

            def blk(i, s, first):
                pe.wait_ge(w_in[s], 16 * i + 16)
                for c in range(CHUNKS):
                    pe.wait_ge(x_in[s][c], 16 * i + 16)
                    for j in range(c * CHUNK, (c + 1) * CHUNK):
                        mm = tile(s, j, P, first and j == 0, False)
                    mm.then_inc(chunk_used, 1)

            for s in range(SLOTS):
                blk(0, s, s == 0)
            with pe.Fori(1, PAIRS) as i:
                for s in range(SLOTS):
                    blk(i, s, False)
            for k, (row, rows) in enumerate(tail):
                pe.wait_ge(x_in[0][k], 16 * PAIRS + 32)
                tile(0, k, rows, False, k == len(tail) - 1)

        @block.vector
        def _(dve):
            nc.vector.memset(w_sb[:, :, :, L:N], 1.0).then_inc(ones_set, 1)
            for b in range(BT):
                dve.wait_ge(bank_full, b + 1)
                s = acc[:, b, L:N]
                nc.vector.tensor_copy(scale[:, b, 0:1], s).then_inc(step_done, 1)
                dve.wait_ge(step_done, 3 * b + 1)
                nc.vector.scalar_tensor_tensor(out=scale[:, b, 1:2], in0=scale[:, b, 0:1], scalar=0.0,
                                               in1=scale[:, b, 0:1],
                                               op0=ALU.is_equal, op1=ALU.add).then_inc(step_done, 1)
                dve.wait_ge(step_done, 3 * b + 2)
                nc.vector.reciprocal(scale[:, b, 2:3], scale[:, b, 1:2]).then_inc(step_done, 1)
                dve.wait_ge(step_done, 3 * b + 3)
                nc.vector.tensor_scalar(y[:, b, :], acc[:, b, 0:L], scale[:, b, 2:3], None,
                                        ALU.mult).then_inc(y_ready, 1)


def kernel(r_entity_idxs, L0_rec_W):
    import numpy as np
    import concourse.bacc as bacc
    from concourse.bass_utils import run_bass_kernel_spmd

    nc = bacc.Bacc("TRN2", target_bir_lowering=False, num_devices=1)
    arrays = {"x_t": np.ascontiguousarray(np.asarray(r_entity_idxs).T),
              "w_t": np.ascontiguousarray(np.asarray(L0_rec_W).T)}
    x_t = nc.dram_tensor("x_t", arrays["x_t"].shape, F32, kind="ExternalInput").ap()
    w_t = nc.dram_tensor("w_t", arrays["w_t"].shape, F32, kind="ExternalInput").ap()
    out = nc.dram_tensor("out", (x_t.shape[1], w_t.shape[1]), F32, kind="ExternalOutput").ap()
    rec_kernel(nc, x_t, w_t, out)
    result = run_bass_kernel_spmd(nc, [arrays], core_ids=[0])
    return result.results[0]["out"]
```

```python
from contextlib import ExitStack

import concourse.bass as bass
from concourse import mybir

F32 = mybir.dt.float32
BF16 = mybir.dt.bfloat16
U16 = mybir.dt.uint16
I32 = mybir.dt.int32
ALU = mybir.AluOpType
ACT = mybir.ActivationFunctionType
AX = mybir.AxisListType

P = 128
T = 8
CHUNK = 2
CHUNKS = T // CHUNK
SLOTS = 2
LOW, TOP = 0, 1
PARTS = 3
PIECE = 2


def rec_kernel(nc, x_t, w_t, out):
    E, B = x_t.shape
    L = w_t.shape[1]
    BANKS = B // P
    PIECES = BANKS // PIECE
    BLOCKS = E // (P * T)
    main = BLOCKS * P * T
    tail = [(r, min(P, E - r)) for r in range(main, E, P)]
    TAIL = len(tail)
    ONES = PARTS * L
    N = ONES + 1
    CHECKS = BLOCKS * CHUNKS + PIECES * TAIL
    assert BLOCKS % 2 == 0 and BLOCKS >= 4 and 0 < TAIL < T and N < 512 and B % (P * PIECE) == 0

    x_blocks = x_t[0:main, :].rearrange("(n p j) b -> n p (j b)", p=P, j=T)
    w_blocks = w_t[0:main, :].rearrange("(n p j) l -> n p (j l)", p=P, j=T)

    with ExitStack() as ctx:
        def sb(name, shape, dt):
            return ctx.enter_context(nc.sbuf_tensor(name, shape, dt))

        def sem(name):
            return ctx.enter_context(nc.semaphore(name))

        x_sb = sb("x_sb", [P, SLOTS, T, B], F32)
        w_raw = sb("w_raw", [P, SLOTS, T, L], F32)
        w_rest = sb("w_rest", [P, T, L], F32)
        w_parts = sb("w_parts", [P, SLOTS, T, N], BF16)
        low_max = sb("low_max", [P, CHECKS], F32)
        act_out = sb("act_out", [P, 2, CHUNK, B], BF16)
        any_low = sb("any_low", [P, 1], BF16)
        one = sb("one", [P, 1], BF16)
        inexact = sb("inexact", [1, 1], I32)
        row_sum = sb("row_sum", [P, BANKS, 3], F32)
        y_sum = sb("y_sum", [P, BANKS, L], F32)
        y = sb("y", [P, BANKS, L], F32)
        w_full = sb("w_full", [P, SLOTS, T, L + 1], F32)
        acc = ctx.enter_context(nc.psum_tensor("acc", [P, BANKS, 512], F32))

        x_halves = x_sb[:, :, :, :].bitcast(BF16).rearrange("p s j (b h) -> p s j b h", h=2)
        x_words = x_sb[:, :, :, :].bitcast(U16).rearrange("p s j (b h) -> p s j b h", h=2)
        w_top = w_raw[:, :, :, :].bitcast(BF16).rearrange("p s j (l h) -> p s j l h", h=2)[:, :, :, :, TOP]
        rest_top = w_rest[:, :, :].bitcast(BF16).rearrange("p j (l h) -> p j l h", h=2)[:, :, :, TOP]

        def part(s, tiles, k):
            return w_parts[:, s, 0:tiles, k * L:(k + 1) * L]

        ones_set = sem("ones_set")
        x_in = [[sem(f"x_in_{s}_{c}") for c in range(CHUNKS)] for s in range(SLOTS)]
        w_in = [sem(f"w_in_{s}") for s in range(SLOTS)]
        tail_in = [sem(f"tail_in_{q}") for q in range(PIECES)]
        hi_done = sem("hi_done")
        rest_done = sem("rest_done")
        mid_done = sem("mid_done")
        split_done = sem("split_done")
        products_done = sem("products_done")
        dve_checked = sem("dve_checked")
        act_checked = sem("act_checked")
        tail_checked = sem("tail_checked")
        bank_full = sem("bank_full")
        lo_out = sem("lo_out")
        mid_added = sem("mid_added")
        sum_step = sem("sum_step")
        y_summed = sem("y_summed")
        y_ready = sem("y_ready")
        y_out = sem("y_out")
        low_known = sem("low_known")
        low_summed = sem("low_summed")
        path_known = sem("path_known")
        full_in = [sem(f"full_in_{s}") for s in range(SLOTS)]
        full_used = sem("full_used")
        full_bank = sem("full_bank")
        full_step = sem("full_step")
        full_ready = sem("full_ready")
        full_out = sem("full_out")
        block = ctx.enter_context(nc.Block())

        @block.gpsimd
        def _(pool):
            nc.gpsimd.memset(w_parts[:, :, :, ONES:N], 1.0)
            nc.gpsimd.memset(w_full[:, :, :, L:L + 1], 1.0)
            nc.gpsimd.memset(one[:, :], 1.0)
            nc.gpsimd.memset(low_max[:, :], 0.0).then_inc(ones_set, 1)

        @block.sync
        def _(sp):
            def load_w(n, s):
                sp.dma_start(w_raw[:, s, :, :].rearrange("p j l -> p (j l)"), w_blocks[n]).then_inc(w_in[s], 16)

            def load_x(n, s, c):
                sp.dma_start(x_sb[:, s, c * CHUNK:(c + 1) * CHUNK, :].rearrange("p j b -> p (j b)"),
                             x_blocks[n, :, c * CHUNK * B:(c + 1) * CHUNK * B]).then_inc(x_in[s][c], 16)

            def free_chunk(n, c):
                sp.wait_ge(products_done, n * CHUNKS + c + 1)
                sp.wait_ge(act_checked if c % 2 else dve_checked, n * CHUNKS + c + 1)

            def refill(n, s):
                for c in range(CHUNKS):
                    free_chunk(n - SLOTS, c)
                    load_x(n, s, c)

            load_w(0, 0)
            load_w(1, 1)
            for c in range(CHUNKS):
                load_x(0, 0, c)
            sp.wait_ge(split_done, 1)
            load_w(2, 0)
            for c in range(CHUNKS):
                load_x(1, 1, c)
            with sp.Fori(1, BLOCKS // 2 - 1) as i:
                for s in range(SLOTS):
                    n = 2 * i + s
                    sp.wait_ge(split_done, n)
                    load_w(n + 1, 1 - s)
                    refill(n, s)
            sp.wait_ge(split_done, BLOCKS - 2)
            load_w(BLOCKS - 1, 1)
            refill(BLOCKS - 2, 0)
            sp.wait_ge(split_done, BLOCKS - 1)
            for k, (row, rows) in enumerate(tail):
                sp.dma_start(w_raw[0:rows, 0, k, :], w_t[row:row + rows, :]).then_inc(w_in[0], 16)
            refill(BLOCKS - 1, 1)
            free_chunk(BLOCKS - 2, CHUNKS - 2)
            free_chunk(BLOCKS - 2, CHUNKS - 1)
            for q in range(PIECES):
                users = slice(q * PIECE * P, (q + 1) * PIECE * P)
                for k, (row, rows) in enumerate(tail):
                    sp.dma_start(x_sb[0:rows, 0, k, users], x_t[row:row + rows, users]).then_inc(tail_in[q], 16)

            for q in range(PIECES):
                sp.wait_ge(y_ready, (q + 1) * PIECE)
                sp.dma_start(out[q * PIECE * P:(q + 1) * PIECE * P, :].rearrange("(b p) l -> p b l", p=P),
                             y[:, q * PIECE:(q + 1) * PIECE, :]).then_inc(y_out, 16)

            sp.wait_ge(path_known, 1)
            with sp.If(sp.value_load(inexact[0:1, 0:1], min_val=0, max_val=1) != 0):
                def load_full(n, s):
                    sp.dma_start(w_full[:, s, :, 0:L], w_blocks[n].rearrange("p (j l) -> p j l", j=T)).then_inc(
                        full_in[s], 16)
                    sp.dma_start(x_sb[:, s, :, :].rearrange("p j b -> p (j b)"), x_blocks[n]).then_inc(
                        full_in[s], 16)

                load_full(0, 0)
                load_full(1, 1)
                with sp.Fori(1, BLOCKS // 2) as i:
                    for s in range(SLOTS):
                        sp.wait_ge(full_used, 2 * i + s - 1)
                        load_full(2 * i + s, s)
                sp.wait_ge(full_used, BLOCKS - 1)
                for k, (row, rows) in enumerate(tail):
                    sp.dma_start(w_full[0:rows, 0, k, 0:L], w_t[row:row + rows, :]).then_inc(full_in[0], 16)
                    sp.dma_start(x_sb[0:rows, 0, k, :], x_t[row:row + rows, :]).then_inc(full_in[0], 16)
                sp.wait_ge(y_out, 16 * PIECES)
                sp.wait_ge(full_ready, BANKS)
                sp.dma_start(out.rearrange("(b p) l -> p b l", p=P), y[:, :, :]).then_inc(full_out, 16)
                sp.wait_ge(full_out, 16)
            sp.wait_ge(y_out, 16 * PIECES)

        @block.scalar
        def _(act):
            def hi(tiles, s):
                nc.scalar.activation(part(s, tiles, 0), w_top[:, s, 0:tiles, :], ACT.Copy).then_inc(hi_done, 1)

            def mid(tiles, n, s):
                act.wait_ge(rest_done, n + 1)
                nc.scalar.activation(part(s, tiles, 1), rest_top[:, 0:tiles, :], ACT.Copy).then_inc(mid_done, 1)

            def check(n, s, c, turn):
                if not isinstance(n, int) or n > 0:
                    act.wait_ge(act_checked, n * CHUNKS + c - 3)
                act.wait_ge(x_in[s][c], 16 * turn + 16)
                nc.scalar.activation(act_out[:, c // 2],
                                     x_words[:, s, c * CHUNK:(c + 1) * CHUNK, :, LOW], ACT.Copy,
                                     accum_out=low_max[:, bass.ds(n * CHUNKS + c, 1)]).then_inc(act_checked, 2)

            def scale_piece(q):
                act.wait_ge(y_summed, q + 1)
                for b in range(q * PIECE, (q + 1) * PIECE):
                    nc.scalar.activation(y[:, b, :], y_sum[:, b, :], ACT.Copy,
                                         scale=row_sum[:, b, 2:3]).then_inc(y_ready, 1)

            def block_step(n, s, turn, tiles, w_bytes_in):
                act.wait_ge(w_in[1 - s], w_bytes_in)
                act.wait_ge(products_done, n * CHUNKS)
                hi(tiles, 1 - s)
                check(n, s, 1, turn)
                mid(tiles, n + 1, 1 - s)
                check(n, s, 3, turn)

            act.wait_ge(w_in[0], 16)
            hi(T, 0)
            mid(T, 0, 0)
            act.wait_ge(ones_set, 1)
            act.wait_ge(w_in[1], 16)
            hi(T, 1)
            check(0, 0, 1, 0)
            mid(T, 1, 1)
            check(0, 0, 3, 0)
            with act.Fori(0, BLOCKS // 2 - 1) as i:
                block_step(2 * i + 1, 1, i, T, 16 * (i + 1) + 16)
                block_step(2 * i + 2, 0, i + 1, T, 16 * (i + 1) + 16)
            block_step(BLOCKS - 1, 1, BLOCKS // 2 - 1, TAIL, 16 * (BLOCKS // 2) + 16 * TAIL)

            for q in range(PIECES):
                banks = slice(q * PIECE, (q + 1) * PIECE)
                act.wait_ge(bank_full, (q + 1) * PIECE)
                nc.scalar.activation(y_sum[:, banks, :], acc[:, banks, 2 * L:3 * L], ACT.Copy).then_inc(lo_out, 1)
                if q:
                    scale_piece(q - 1)
            scale_piece(PIECES - 1)

        @block.vector
        def _(dve):
            def rest(tiles, n, s):
                dve.wait_ge(hi_done, n + 1)
                nc.vector.tensor_tensor(w_rest[:, 0:tiles, :], w_raw[:, s, 0:tiles, :], part(s, tiles, 0),
                                        ALU.subtract).then_inc(rest_done, 1)

            def lo(tiles, n, s):
                dve.wait_ge(mid_done, n + 1)
                nc.vector.tensor_tensor(part(s, tiles, 2), w_rest[:, 0:tiles, :], part(s, tiles, 1),
                                        ALU.subtract).then_inc(split_done, 1)

            def check(n, s, c, turn):
                dve.wait_ge(x_in[s][c], 16 * turn + 16)
                nc.vector.tensor_reduce(low_max[:, bass.ds(n * CHUNKS + c, 1)],
                                        x_words[:, s, c * CHUNK:(c + 1) * CHUNK, :, LOW], AX.XY,
                                        ALU.max).then_inc(dve_checked, 2)

            def block_step(n, s, turn, tiles):
                dve.wait_ge(split_done, n + 1)
                rest(tiles, n + 1, 1 - s)
                check(n, s, 0, turn)
                lo(tiles, n + 1, 1 - s)
                check(n, s, 2, turn)

            rest(T, 0, 0)
            lo(T, 0, 0)
            dve.wait_ge(ones_set, 1)
            block_step(0, 0, 0, T)
            with dve.Fori(0, BLOCKS // 2 - 1) as i:
                block_step(2 * i + 1, 1, i, T)
                block_step(2 * i + 2, 0, i + 1, T)
            block_step(BLOCKS - 1, 1, BLOCKS // 2 - 1, TAIL)

            for q in range(PIECES):
                banks = slice(q * PIECE, (q + 1) * PIECE)
                dve.wait_ge(tail_in[q], 16 * TAIL)
                for k, (row, rows) in enumerate(tail):
                    col = BLOCKS * CHUNKS + q * TAIL + k
                    nc.vector.tensor_reduce(low_max[0:rows, col:col + 1],
                                            x_words[0:rows, 0, k, q * PIECE * P:(q + 1) * PIECE * P, LOW], AX.X,
                                            ALU.max).then_inc(tail_checked, 1)
                dve.wait_ge(bank_full, (q + 1) * PIECE)
                dve.wait_ge(lo_out, q + 1)
                nc.vector.tensor_scalar(row_sum[:, banks, 0], acc[:, banks, ONES], 0.0, None,
                                        ALU.is_equal).then_inc(sum_step, 1)
                nc.vector.tensor_tensor(y_sum[:, banks, :], acc[:, banks, L:2 * L], y_sum[:, banks, :],
                                        ALU.add).then_inc(mid_added, 1)
                dve.wait_ge(sum_step, 2 * q + 1)
                nc.vector.tensor_tensor(row_sum[:, banks, 1], acc[:, banks, ONES], row_sum[:, banks, 0],
                                        ALU.add).then_inc(sum_step, 1)
                dve.wait_ge(sum_step, 2 * q + 2)
                nc.vector.reciprocal(row_sum[:, banks, 2], row_sum[:, banks, 1])
                dve.wait_ge(mid_added, q + 1)
                nc.vector.tensor_tensor(y_sum[:, banks, :], acc[:, banks, 0:L], y_sum[:, banks, :],
                                        ALU.add).then_inc(y_summed, 1)

            dve.wait_ge(act_checked, BLOCKS * CHUNKS)
            dve.wait_ge(dve_checked, BLOCKS * CHUNKS)
            dve.wait_ge(tail_checked, PIECES * TAIL)
            nc.vector.tensor_reduce(any_low[:, :], low_max[:, :], AX.X, ALU.max).then_inc(low_known, 1)
            dve.wait_ge(low_summed, 1)
            nc.vector.tensor_scalar(inexact[0:1, 0:1], acc[0:1, 0, N:N + 1], 0.0, None,
                                    ALU.is_gt).then_inc(path_known, 1)
            dve.wait_ge(path_known, 1)
            with dve.If(dve.value_load(inexact[0:1, 0:1], min_val=0, max_val=1) != 0):
                dve.wait_ge(y_out, 16 * PIECES)
                for b in range(BANKS):
                    dve.wait_ge(full_bank, b + 1)
                    nc.vector.tensor_scalar(row_sum[:, b, 0:1], acc[:, b, L:L + 1], 0.0, None,
                                            ALU.is_equal).then_inc(full_step, 1)
                    dve.wait_ge(full_step, 3 * b + 1)
                    nc.vector.tensor_tensor(row_sum[:, b, 1:2], acc[:, b, L:L + 1], row_sum[:, b, 0:1],
                                            ALU.add).then_inc(full_step, 1)
                    dve.wait_ge(full_step, 3 * b + 2)
                    nc.vector.reciprocal(row_sum[:, b, 2:3], row_sum[:, b, 1:2]).then_inc(full_step, 1)
                    dve.wait_ge(full_step, 3 * b + 3)
                    nc.vector.tensor_scalar(y[:, b, :], acc[:, b, 0:L], row_sum[:, b, 2:3], None,
                                            ALU.mult).then_inc(full_ready, 1)

        @block.tensor
        def _(pe):
            def product(s, j, rows, b, first, last):
                return nc.tensor.matmul(acc[:, b, 0:N], x_halves[0:rows, s, j, b * P:(b + 1) * P, TOP],
                                        w_parts[0:rows, s, j, :], start=first, stop=last)

            def multiply(n, s, turn, first):
                pe.wait_ge(split_done, n + 1)
                for c in range(CHUNKS):
                    pe.wait_ge(x_in[s][c], 16 * turn + 16)
                    for j in range(c * CHUNK, (c + 1) * CHUNK):
                        for b in range(BANKS):
                            mm = product(s, j, P, b, first and j == 0, False)
                    mm.then_inc(products_done, 1)

            pe.wait_ge(ones_set, 1)
            multiply(0, 0, 0, True)
            multiply(1, 1, 0, False)
            with pe.Fori(1, BLOCKS // 2) as i:
                for s in range(SLOTS):
                    multiply(2 * i + s, s, i, False)
            pe.wait_ge(split_done, BLOCKS + 1)
            for q in range(PIECES):
                pe.wait_ge(tail_in[q], 16 * TAIL)
                for b in range(q * PIECE, (q + 1) * PIECE):
                    for k, (row, rows) in enumerate(tail):
                        mm = product(0, k, rows, b, False, k == TAIL - 1)
                    mm.then_inc(bank_full, 1)

            pe.wait_ge(low_known, 1)
            nc.tensor.matmul(acc[0:1, 0, N:N + 1], any_low[:, :], one[:, :], start=True,
                             stop=True).then_inc(low_summed, 1)
            pe.wait_ge(path_known, 1)
            with pe.If(pe.value_load(inexact[0:1, 0:1], min_val=0, max_val=1) != 0):
                def product_full(s, j, rows, b, first, last):
                    return nc.tensor.matmul(acc[:, b, 0:L + 1], x_sb[0:rows, s, j, b * P:(b + 1) * P],
                                            w_full[0:rows, s, j, :], start=first, stop=last)

                def multiply_full(s, turn, first):
                    pe.wait_ge(full_in[s], 32 * turn + 32)
                    for j in range(T):
                        for b in range(BANKS):
                            mm = product_full(s, j, P, b, first and j == 0, False)
                    mm.then_inc(full_used, 1)

                multiply_full(0, 0, True)
                multiply_full(1, 0, False)
                with pe.Fori(1, BLOCKS // 2) as i:
                    for s in range(SLOTS):
                        multiply_full(s, i, False)
                pe.wait_ge(full_in[0], 32 * (BLOCKS // 2) + 32 * TAIL)
                for b in range(BANKS):
                    for k, (row, rows) in enumerate(tail):
                        mm = product_full(0, k, rows, b, False, k == TAIL - 1)
                    mm.then_inc(full_bank, 1)


def kernel(r_entity_idxs, L0_rec_W):
    import numpy as np
    import concourse.bacc as bacc
    from concourse.bass_utils import run_bass_kernel_spmd

    nc = bacc.Bacc("TRN2", target_bir_lowering=False, num_devices=1)
    arrays = {"x_t": np.ascontiguousarray(np.asarray(r_entity_idxs).T),
              "w_t": np.ascontiguousarray(np.asarray(L0_rec_W).T)}
    x_t = nc.dram_tensor("x_t", arrays["x_t"].shape, F32, kind="ExternalInput").ap()
    w_t = nc.dram_tensor("w_t", arrays["w_t"].shape, F32, kind="ExternalInput").ap()
    out = nc.dram_tensor("out", (x_t.shape[1], w_t.shape[1]), F32, kind="ExternalOutput").ap()
    rec_kernel(nc, x_t, w_t, out)
    result = run_bass_kernel_spmd(nc, [arrays], core_ids=[0])
    return result.results[0]["out"]
```

```python
from contextlib import ExitStack

import concourse.bass as bass
from concourse import mybir

F32 = mybir.dt.float32
BF16 = mybir.dt.bfloat16
U16 = mybir.dt.uint16
I32 = mybir.dt.int32
ALU = mybir.AluOpType
ACT = mybir.ActivationFunctionType
AX = mybir.AxisListType

P = 128
T = 8
CHUNK = 2
CHUNKS = T // CHUNK
SLOTS = 2
LOW, TOP = 0, 1
PARTS = 3
PIECE = 2


def rec_kernel(nc, x_t, w_t, out):
    E, B = x_t.shape
    L = w_t.shape[1]
    BANKS = B // P
    PIECES = BANKS // PIECE
    USERS = PIECE * P
    BLOCKS = E // (P * T)
    head_rows = E - BLOCKS * P * T
    head = [(r, min(P, head_rows - r)) for r in range(0, head_rows, P)]
    HEAD = len(head)
    ONES = PARTS * L
    N = ONES + 1
    LOADS = [(q, 0, T) for q in range(PIECES - 2)]
    LOADS += [(PIECES - 2, j, j + T // 2) for j in range(0, T, T // 2)]
    LOADS += [(PIECES - 1, j, j + CHUNK) for j in range(0, T, CHUNK)]
    LAST_COL = BLOCKS * CHUNKS
    CHECKS = LAST_COL + 2 * len(LOADS)
    assert BLOCKS % 2 == 0 and BLOCKS >= 4 and HEAD == 2 and N < 512 and B % USERS == 0

    x_blocks = x_t[head_rows:E, :].rearrange("(n p j) b -> n p j b", p=P, j=T)
    w_blocks = w_t[head_rows:E, :].rearrange("(n p j) l -> n p j l", p=P, j=T)

    with ExitStack() as ctx:
        def sb(name, shape, dt):
            return ctx.enter_context(nc.sbuf_tensor(name, shape, dt))

        def sem(name):
            return ctx.enter_context(nc.semaphore(name))

        x_sb = sb("x_sb", [P, SLOTS, T, B], F32)
        w_raw = sb("w_raw", [P, SLOTS, T, L], F32)
        w_rest = sb("w_rest", [P, T, L], F32)
        w_parts = sb("w_parts", [P, SLOTS, T, N], BF16)
        low_max = sb("low_max", [P, CHECKS], F32)
        act_out = sb("act_out", [P, 2, CHUNK * B], BF16)
        any_low = sb("any_low", [P, 1], BF16)
        one = sb("one", [P, 1], BF16)
        inexact = sb("inexact", [1, 1], I32)
        row_sum = sb("row_sum", [P, BANKS, 3], F32)
        y_sum = sb("y_sum", [P, BANKS, L], F32)
        y = sb("y", [P, BANKS, L], F32)
        w_full = sb("w_full", [P, SLOTS, T, L + 1], F32)
        acc = ctx.enter_context(nc.psum_tensor("acc", [P, BANKS, 512], F32))

        x_top = x_sb[:, :, :, :].bitcast(BF16).rearrange("p s j (b h) -> p s j b h", h=2)[:, :, :, :, TOP]
        x_low = x_sb[:, :, :, :].bitcast(U16).rearrange("p s j (b h) -> p s j b h", h=2)[:, :, :, :, LOW]
        w_top = w_raw[:, :, :, :].bitcast(BF16).rearrange("p s j (l h) -> p s j l h", h=2)[:, :, :, :, TOP]
        rest_top = w_rest[:, :, :].bitcast(BF16).rearrange("p j (l h) -> p j l h", h=2)[:, :, :, TOP]

        def part(s, k, rows=P, tiles=slice(0, T)):
            return w_parts[0:rows, s, tiles, k * L:(k + 1) * L]

        WHOLE = [(P, slice(0, T))]
        SHORT = [(rows, slice(k, k + 1)) for k, (_, rows) in enumerate(head)]

        def chunk(c):
            return slice(c * CHUNK, (c + 1) * CHUNK)

        def users(q):
            return slice(q * USERS, (q + 1) * USERS)

        def bank(b):
            return slice(b * P, (b + 1) * P)

        x_in = [[sem(f"x_in_{s}_{c}") for c in range(CHUNKS)] for s in range(SLOTS)]
        w_in = [sem(f"w_in_{s}") for s in range(SLOTS)]
        x_head_in = [sem(f"x_head_in_{k}") for k in range(HEAD)]
        w_head_in = sem("w_head_in")
        last_in = [sem(f"last_in_{k}") for k in range(len(LOADS))]
        ones_set = sem("ones_set")
        hi_done = sem("hi_done")
        rest_done = sem("rest_done")
        mid_done = sem("mid_done")
        split_done = sem("split_done")
        products_done = sem("products_done")
        dve_checked = sem("dve_checked")
        act_checked = sem("act_checked")
        bank_full = sem("bank_full")
        lo_out = sem("lo_out")
        mid_added = sem("mid_added")
        sum_step = sem("sum_step")
        inverse_done = sem("inverse_done")
        y_summed = sem("y_summed")
        y_ready = sem("y_ready")
        y_out = sem("y_out")
        low_known = sem("low_known")
        low_summed = sem("low_summed")
        path_known = sem("path_known")
        full_in = [sem(f"full_in_{s}") for s in range(SLOTS)]
        full_used = sem("full_used")
        full_bank = sem("full_bank")
        full_step = sem("full_step")
        full_ready = sem("full_ready")
        full_out = sem("full_out")
        block = ctx.enter_context(nc.Block())

        @block.gpsimd
        def _(pool):
            nc.gpsimd.memset(w_parts[:, :, :, ONES:N], 1.0)
            nc.gpsimd.memset(w_full[:, :, :, L:L + 1], 1.0)
            nc.gpsimd.memset(one[:, :], 1.0)
            nc.gpsimd.memset(low_max[:, :], 0.0).then_inc(ones_set, 1)

        @block.sync
        def _(sp):
            def load_w(m, s):
                sp.dma_start(w_raw[:, s, :, :].rearrange("p j l -> p (j l)"),
                             w_blocks[m - 1].rearrange("p j l -> p (j l)")).then_inc(w_in[s], 16)

            def load_x(m, s, c):
                sp.dma_start(x_sb[:, s, chunk(c), :].rearrange("p j b -> p (j b)"),
                             x_blocks[m - 1, :, chunk(c), :].rearrange("p j b -> p (j b)")).then_inc(x_in[s][c], 16)

            def free_chunk(m, c):
                sp.wait_ge(products_done, m * CHUNKS + c + 1)
                sp.wait_ge(act_checked if c % 2 else dve_checked, m * CHUNKS + c + 1)

            def load_x_head(k):
                row, rows = head[k]
                sp.dma_start(x_sb[0:rows, 0, k, :], x_t[row:row + rows, :]).then_inc(x_head_in[k], 16)

            load_x_head(0)
            for k, (row, rows) in enumerate(head):
                sp.dma_start(w_raw[0:rows, 0, k, :], w_t[row:row + rows, :]).then_inc(w_head_in, 16)
            load_x_head(1)
            load_w(1, 1)
            load_x(1, 1, 0)
            load_x(1, 1, 1)
            sp.wait_ge(split_done, 1)
            load_w(2, 0)
            load_x(1, 1, 2)
            load_x(1, 1, 3)
            with sp.Fori(1, BLOCKS // 2) as i:
                for s in range(SLOTS):
                    m = 2 * i + s
                    sp.wait_ge(split_done, m)
                    load_w(m + 1, 1 - s)
                    for c in range(CHUNKS):
                        free_chunk(m - SLOTS, c)
                        load_x(m, s, c)
            for c in range(CHUNKS):
                free_chunk(BLOCKS - SLOTS, c)
            for k, (q, j, end) in enumerate(LOADS):
                sp.dma_start(x_sb[:, 0, j:end, users(q)],
                             x_blocks[BLOCKS - 1, :, j:end, users(q)]).then_inc(last_in[k], 16)

            for q in range(PIECES):
                sp.wait_ge(y_ready, (q + 1) * PIECE)
                sp.dma_start(out[users(q), :].rearrange("(b p) l -> p b l", p=P),
                             y[:, q * PIECE:(q + 1) * PIECE, :]).then_inc(y_out, 16)

            sp.wait_ge(path_known, 1)
            with sp.If(sp.value_load(inexact[0:1, 0:1], min_val=0, max_val=1) != 0):
                def load_full(n, s):
                    sp.dma_start(w_full[:, s, :, 0:L], w_blocks[n]).then_inc(full_in[s], 16)
                    sp.dma_start(x_sb[:, s, :, :], x_blocks[n]).then_inc(full_in[s], 16)

                load_full(0, 0)
                load_full(1, 1)
                with sp.Fori(1, BLOCKS // 2) as i:
                    for s in range(SLOTS):
                        sp.wait_ge(full_used, 2 * i + s - 1)
                        load_full(2 * i + s, s)
                sp.wait_ge(full_used, BLOCKS - 1)
                for k, (row, rows) in enumerate(head):
                    sp.dma_start(w_full[0:rows, 0, k, 0:L], w_t[row:row + rows, :]).then_inc(full_in[0], 16)
                    sp.dma_start(x_sb[0:rows, 0, k, :], x_t[row:row + rows, :]).then_inc(full_in[0], 16)
                sp.wait_ge(y_out, 16 * PIECES)
                sp.wait_ge(full_ready, BANKS)
                sp.dma_start(out.rearrange("(b p) l -> p b l", p=P), y[:, :, :]).then_inc(full_out, 16)
                sp.wait_ge(full_out, 16)
            sp.wait_ge(y_out, 16 * PIECES)

        @block.scalar
        def _(act):
            def hi(s, shape=WHOLE):
                for rows, tiles in shape:
                    op = nc.scalar.activation(part(s, 0, rows, tiles), w_top[0:rows, s, tiles, :], ACT.Copy)
                op.then_inc(hi_done, 1)

            def mid(m, s, shape=WHOLE):
                act.wait_ge(rest_done, m + 1)
                for rows, tiles in shape:
                    op = nc.scalar.activation(part(s, 1, rows, tiles), rest_top[0:rows, tiles, :], ACT.Copy)
                op.then_inc(mid_done, 1)

            def low_sum(low, rows, buf, col, count):
                tiles, n = low.shape[1:]
                nc.scalar.activation(act_out[0:rows, buf, 0:tiles * n].rearrange("p (j b) -> p j b", j=tiles), low,
                                     ACT.Copy, accum_out=low_max[0:rows, bass.ds(col, 1)]).then_inc(act_checked, count)

            def check(m, s, c, landed):
                act.wait_ge(act_checked, m * CHUNKS + c - 3)
                act.wait_ge(x_in[s][c], landed)
                low_sum(x_low[:, s, chunk(c), :], P, c // 2, m * CHUNKS + c, 2)

            def step(m, s, x_landed, w_landed):
                act.wait_ge(w_in[1 - s], w_landed)
                act.wait_ge(products_done, m * CHUNKS)
                hi(1 - s)
                check(m, s, 1, x_landed)
                mid(m + 1, 1 - s)
                check(m, s, 3, x_landed)

            act.wait_ge(w_head_in, 16 * HEAD)
            hi(0, SHORT)
            mid(0, 0, SHORT)
            act.wait_ge(ones_set, 1)
            act.wait_ge(x_head_in[1], 16)
            low_sum(x_low[0:head[1][1], 0, 1:2, :], head[1][1], 0, 1, CHUNKS)
            act.wait_ge(w_in[1], 16)
            hi(1)
            mid(1, 1)
            with act.Fori(0, BLOCKS // 2 - 1) as i:
                step(2 * i + 1, 1, 16 * (i + 1), 16 * (i + 1))
                step(2 * i + 2, 0, 16 * (i + 1), 16 * (i + 2))
            step(BLOCKS - 1, 1, 16 * (BLOCKS // 2), 16 * (BLOCKS // 2))

            def lo_to_sbuf(b):
                act.wait_ge(bank_full, b + 1)
                nc.scalar.activation(y_sum[:, b, :], acc[:, b, 2 * L:3 * L], ACT.Copy).then_inc(lo_out, 1)

            def scale(b):
                act.wait_ge(y_summed, b + 1)
                act.wait_ge(inverse_done, b // PIECE + 1)
                nc.scalar.activation(y[:, b, :], y_sum[:, b, :], ACT.Copy,
                                     scale=row_sum[:, b, 2:3]).then_inc(y_ready, 1)

            def check_last(k):
                q, j, end = LOADS[k]
                act.wait_ge(act_checked, LAST_COL - 1 + k if k else LAST_COL - 2)
                act.wait_ge(last_in[k], 16)
                low_sum(x_low[:, 0, j:end, bank(q * PIECE + 1)], P, k % 2, LAST_COL + 2 * k + 1, 1)

            for k, (q, j, end) in enumerate(LOADS):
                if k < len(LOADS) - 1:
                    check_last(k)
                if j == 0 and q:
                    scale((q - 1) * PIECE)
                if end == T:
                    for b in range(q * PIECE, (q + 1) * PIECE):
                        lo_to_sbuf(b)
            scale(BANKS - PIECE)
            check_last(len(LOADS) - 1)

        @block.vector
        def _(dve):
            def rest(m, s, shape=WHOLE):
                dve.wait_ge(hi_done, m + 1)
                for rows, tiles in shape:
                    op = nc.vector.tensor_tensor(w_rest[0:rows, tiles, :], w_raw[0:rows, s, tiles, :],
                                                 part(s, 0, rows, tiles), ALU.subtract)
                op.then_inc(rest_done, 1)

            def lo(m, s, shape=WHOLE):
                dve.wait_ge(mid_done, m + 1)
                for rows, tiles in shape:
                    op = nc.vector.tensor_tensor(part(s, 2, rows, tiles), w_rest[0:rows, tiles, :],
                                                 part(s, 1, rows, tiles), ALU.subtract)
                op.then_inc(split_done, 1)

            def low_largest(low, rows, col, count):
                nc.vector.tensor_reduce(low_max[0:rows, bass.ds(col, 1)], low, AX.XY, ALU.max).then_inc(
                    dve_checked, count)

            def check(m, s, c, landed):
                dve.wait_ge(x_in[s][c], landed)
                low_largest(x_low[:, s, chunk(c), :], P, m * CHUNKS + c, 2)

            def step(m, s, x_landed):
                dve.wait_ge(split_done, m + 1)
                rest(m + 1, 1 - s)
                check(m, s, 0, x_landed)
                lo(m + 1, 1 - s)
                check(m, s, 2, x_landed)

            rest(0, 0, SHORT)
            lo(0, 0, SHORT)
            dve.wait_ge(ones_set, 1)
            dve.wait_ge(x_head_in[0], 16)
            low_largest(x_low[0:head[0][1], 0, 0:1, :], head[0][1], 0, CHUNKS)
            dve.wait_ge(split_done, 1)
            rest(1, 1)
            lo(1, 1)
            with dve.Fori(0, BLOCKS // 2 - 1) as i:
                step(2 * i + 1, 1, 16 * (i + 1))
                step(2 * i + 2, 0, 16 * (i + 1))
            step(BLOCKS - 1, 1, 16 * (BLOCKS // 2))

            def row_sum_is_zero(q, col):
                banks = slice(q * PIECE, (q + 1) * PIECE)
                return nc.vector.tensor_scalar(row_sum[:, banks, 0], acc[:, banks, col], 0.0, None, ALU.is_equal)

            def safe_row_sum(q, col):
                banks = slice(q * PIECE, (q + 1) * PIECE)
                return nc.vector.tensor_tensor(row_sum[:, banks, 1], acc[:, banks, col], row_sum[:, banks, 0], ALU.add)

            def inverse_row_sum(q):
                banks = slice(q * PIECE, (q + 1) * PIECE)
                return nc.vector.reciprocal(row_sum[:, banks, 2], row_sum[:, banks, 1])

            def add_part(b, k):
                return nc.vector.tensor_tensor(y_sum[:, b, :], acc[:, b, k * L:(k + 1) * L], y_sum[:, b, :], ALU.add)

            def finish(q):
                b, c = q * PIECE, q * PIECE + 1
                dve.wait_ge(lo_out, b + 1)
                add_part(b, 1).then_inc(mid_added, 1)
                dve.wait_ge(lo_out, c + 1)
                row_sum_is_zero(q, ONES).then_inc(sum_step, 1)
                add_part(c, 1).then_inc(mid_added, 1)
                dve.wait_ge(sum_step, 2 * q + 1)
                safe_row_sum(q, ONES).then_inc(sum_step, 1)
                dve.wait_ge(mid_added, b + 1)
                add_part(b, 0).then_inc(y_summed, 1)
                dve.wait_ge(sum_step, 2 * q + 2)
                inverse_row_sum(q).then_inc(inverse_done, 1)
                dve.wait_ge(mid_added, c + 1)
                add_part(c, 0).then_inc(y_summed, 1)
                dve.wait_ge(inverse_done, q + 1)
                dve.wait_ge(y_summed, c + 1)
                nc.vector.tensor_scalar(y[:, c, :], y_sum[:, c, :], row_sum[:, c, 2:3], None,
                                        ALU.mult).then_inc(y_ready, 1)

            def check_last(k):
                q, j, end = LOADS[k]
                dve.wait_ge(last_in[k], 16)
                low_largest(x_low[:, 0, j:end, bank(q * PIECE)], P, LAST_COL + 2 * k, 1)

            for k, (q, j, end) in enumerate(LOADS):
                if k < len(LOADS) - 1:
                    check_last(k)
                if end == T:
                    finish(q)
            check_last(len(LOADS) - 1)

            dve.wait_ge(act_checked, LAST_COL + len(LOADS))
            dve.wait_ge(dve_checked, LAST_COL + len(LOADS))
            nc.vector.tensor_reduce(any_low[:, :], low_max[:, :], AX.X, ALU.max).then_inc(low_known, 1)
            dve.wait_ge(low_summed, 1)
            nc.vector.tensor_scalar(inexact[0:1, 0:1], acc[0:1, 0, N:N + 1], 0.0, None,
                                    ALU.is_gt).then_inc(path_known, 1)
            dve.wait_ge(path_known, 1)
            with dve.If(dve.value_load(inexact[0:1, 0:1], min_val=0, max_val=1) != 0):
                dve.wait_ge(y_out, 16 * PIECES)
                for q in range(PIECES):
                    dve.wait_ge(full_bank, (q + 1) * PIECE)
                    row_sum_is_zero(q, L).then_inc(full_step, 1)
                    dve.wait_ge(full_step, 3 * q + 1)
                    safe_row_sum(q, L).then_inc(full_step, 1)
                    dve.wait_ge(full_step, 3 * q + 2)
                    inverse_row_sum(q).then_inc(full_step, 1)
                    dve.wait_ge(full_step, 3 * q + 3)
                    for b in range(q * PIECE, (q + 1) * PIECE):
                        nc.vector.tensor_scalar(y[:, b, :], acc[:, b, 0:L], row_sum[:, b, 2:3], None,
                                                ALU.mult).then_inc(full_ready, 1)

        @block.tensor
        def _(pe):
            def product(s, j, rows, b, first=False, last=False):
                return nc.tensor.matmul(acc[:, b, 0:N], x_top[0:rows, s, j, b * P:(b + 1) * P],
                                        w_parts[0:rows, s, j, :], start=first, stop=last)

            def step(m, s, x_landed):
                pe.wait_ge(split_done, m + 1)
                for c in range(CHUNKS):
                    pe.wait_ge(x_in[s][c], x_landed)
                    for j in range(c * CHUNK, (c + 1) * CHUNK):
                        for b in range(BANKS):
                            mm = product(s, j, P, b)
                    mm.then_inc(products_done, 1)

            pe.wait_ge(ones_set, 1)
            pe.wait_ge(split_done, 1)
            for k, (row, rows) in enumerate(head):
                pe.wait_ge(x_head_in[k], 16)
                for b in range(BANKS):
                    mm = product(0, k, rows, b, first=k == 0)
            mm.then_inc(products_done, CHUNKS)
            with pe.Fori(0, BLOCKS // 2 - 1) as i:
                step(2 * i + 1, 1, 16 * (i + 1))
                step(2 * i + 2, 0, 16 * (i + 1))
            step(BLOCKS - 1, 1, 16 * (BLOCKS // 2))

            pe.wait_ge(split_done, BLOCKS + 1)
            for k, (q, first, end) in enumerate(LOADS):
                pe.wait_ge(last_in[k], 16)
                for b in range(q * PIECE, (q + 1) * PIECE):
                    for j in range(first, end):
                        mm = product(0, j, P, b, last=j == T - 1)
                    if end == T:
                        mm.then_inc(bank_full, 1)

            pe.wait_ge(low_known, 1)
            nc.tensor.matmul(acc[0:1, 0, N:N + 1], any_low[:, :], one[:, :], start=True,
                             stop=True).then_inc(low_summed, 1)
            pe.wait_ge(path_known, 1)
            with pe.If(pe.value_load(inexact[0:1, 0:1], min_val=0, max_val=1) != 0):
                def product_full(s, j, rows, b, first, last):
                    return nc.tensor.matmul(acc[:, b, 0:L + 1], x_sb[0:rows, s, j, b * P:(b + 1) * P],
                                            w_full[0:rows, s, j, :], start=first, stop=last)

                def multiply_full(s, landed, first):
                    pe.wait_ge(full_in[s], landed)
                    for j in range(T):
                        for b in range(BANKS):
                            mm = product_full(s, j, P, b, first and j == 0, False)
                    mm.then_inc(full_used, 1)

                multiply_full(0, 32, True)
                multiply_full(1, 32, False)
                with pe.Fori(1, BLOCKS // 2) as i:
                    for s in range(SLOTS):
                        multiply_full(s, 32 * i + 32, False)
                pe.wait_ge(full_in[0], 32 * (BLOCKS // 2) + 32 * HEAD)
                for b in range(BANKS):
                    for k, (row, rows) in enumerate(head):
                        mm = product_full(0, k, rows, b, False, k == HEAD - 1)
                    mm.then_inc(full_bank, 1)


def kernel(r_entity_idxs, L0_rec_W):
    import numpy as np
    import concourse.bacc as bacc
    from concourse.bass_utils import run_bass_kernel_spmd

    nc = bacc.Bacc("TRN2", target_bir_lowering=False, num_devices=1)
    arrays = {"x_t": np.ascontiguousarray(np.asarray(r_entity_idxs).T),
              "w_t": np.ascontiguousarray(np.asarray(L0_rec_W).T)}
    x_t = nc.dram_tensor("x_t", arrays["x_t"].shape, F32, kind="ExternalInput").ap()
    w_t = nc.dram_tensor("w_t", arrays["w_t"].shape, F32, kind="ExternalInput").ap()
    out = nc.dram_tensor("out", (x_t.shape[1], w_t.shape[1]), F32, kind="ExternalOutput").ap()
    rec_kernel(nc, x_t, w_t, out)
    result = run_bass_kernel_spmd(nc, [arrays], core_ids=[0])
    return result.results[0]["out"]
```
